# Optimizing a Trainium2 kernel written in Bass

```python
import numpy as np
import jax
import jax.numpy as jnp

def _softmax(x, axis=-1):
    return jax.nn.softmax(x, axis=axis)

def _gelu(x):
    return jax.nn.gelu(x, approximate=True)

def _silu(x):
    return jax.nn.silu(x)

def _sigmoid(x):
    return jax.nn.sigmoid(x)

def _layernorm(x, axis=-1, eps=1e-05):
    m = jnp.mean(x, axis=axis, keepdims=True)
    v = jnp.var(x, axis=axis, keepdims=True)
    return (x - m) / jnp.sqrt(v + eps)

def _scatter_add(tgt, idx, src, axis=0):
    return tgt.at[idx].add(src)

def _segment_sum(src, seg, n):
    return jax.ops.segment_sum(src, seg, n)
kernel_name = 'mk_rec_standalone_d1_rec_r8_047562'

def setup_inputs(seed: int=0):
    np.random.seed(seed)
    _w = jnp.asarray

    def _rec_inputs():
        import jax
        import jax.numpy as jnp
        _rk = jax.random.key(seed)
        r_x = -0.000521161 + 1.00038 * jax.random.normal(jax.random.fold_in(_rk, 1), (2048, 26, 32), jnp.float32)
        return r_x
    r_x = _rec_inputs()

    def _L0_rec_setup():
        import jax, jax.numpy as jnp
        import numpy as np
        FIELD_SIZE = 26
        EMBED_DIM = 32
        _I, _J = np.triu_indices(FIELD_SIZE, k=1)
        NUM_PAIRS = _I.shape[0]
        key = jax.random.key(seed)
        k1, k2, k3 = jax.random.split(key, 3)
        B = 512
        x = jax.random.normal(k1, (B, FIELD_SIZE, EMBED_DIM), dtype=jnp.float32)
        W = jax.random.normal(k2, (NUM_PAIRS, EMBED_DIM, EMBED_DIM), dtype=jnp.float32) * (1.0 / np.sqrt(EMBED_DIM))
        b = jax.random.normal(k3, (NUM_PAIRS, EMBED_DIM), dtype=jnp.float32) * 0.01
        return {'x': x, 'W': W, 'b': b}
    _L0_rec_all = _L0_rec_setup()
    _L0_rec_in = {k: v for k, v in _L0_rec_all.items() if k in ('W', 'b')}
    del _L0_rec_all
    return {'r_x': r_x, 'L0_rec_W': _L0_rec_in['W'], 'L0_rec_b': _L0_rec_in['b']}

def reference(r_x, L0_rec_W, L0_rec_b):
    import jax
    import jax.numpy as jnp

    def _L0_rec_ref(x, W, b):
        import jax, jax.numpy as jnp
        import numpy as np
        FIELD_SIZE = 26
        EMBED_DIM = 32
        _I, _J = np.triu_indices(FIELD_SIZE, k=1)
        NUM_PAIRS = _I.shape[0]
        i_idx = jnp.asarray(_I)
        j_idx = jnp.asarray(_J)
        v_i = x[:, i_idx, :]
        v_j = x[:, j_idx, :]
        t = jnp.einsum('bpd,ped->bpe', v_i, W) + b[None, :, :]
        return t * v_j
    y = _L0_rec_ref(r_x, L0_rec_W, L0_rec_b)
    return y

_drawn_inputs = setup_inputs


def setup_inputs(seed=0):
    import zlib

    import numpy as np

    out = dict(_drawn_inputs(seed))
    spreads = {}
    factors = {'L0_rec_b': 5.587}
    for name, (base, spread) in spreads.items():
        noise = np.random.default_rng([zlib.crc32(name.encode()), seed]).standard_normal(out[name].shape)
        drawn = base * np.exp(spread * noise) if base else spread * noise
        out[name] = jnp.asarray(drawn.astype(out[name].dtype))
    for name, factor in factors.items():
        out[name] = (out[name] * factor).astype(out[name].dtype)
    return out
```

```python
import concourse.bass as bass
from concourse import mybir
from contextlib import ExitStack


def pairwise_bilinear_kernel(nc: bass.Bass, x: bass.AP, W: bass.AP, b: bass.AP, out: bass.AP):
    fp32 = mybir.dt.float32
    bf16 = mybir.dt.bfloat16
    ALU = mybir.AluOpType
    ACT = mybir.ActivationFunctionType

    P = 128
    BATCH, F, D = x.shape
    PAIRS = F * (F - 1) // 2
    TILES = BATCH // P
    COLS = PAIRS * D
    ROWG = P // D
    XG = (F + ROWG - 1) // ROWG
    BANK = 512
    SLOTS = 4

    def npairs(i):
        return F - 1 - i

    x_col = [min(g * P, F * D - P) for g in range(XG)]
    row_group = [(i * D - x_col[i // ROWG]) // D for i in range(F)]
    first_pair = [sum(npairs(k) for k in range(i)) for i in range(F)]
    w_first = [sum(npairs(k) for k in range(i) if row_group[k] == row_group[i]) for i in range(F)]
    W_BLOCKS = max(w_first[i] + npairs(i) for i in range(F))

    VEC, GPS, TRN = "v", "g", "t"
    UNITS = [((i,), GPS if i in (3, 7, 11, 15) else VEC) for i in range(18)]
    UNITS.insert(12, ((), TRN))
    UNITS += [((18, 22), GPS), ((19, 23), VEC), ((20,), VEC), ((21,), VEC), ((24,), VEC)]
    assert len(UNITS) % SLOTS == 0
    NU = len(UNITS)
    vec_upto = [sum(o == VEC for _, o in UNITS[:u + 1]) for u in range(NU)]
    gps_upto = [sum(o == GPS for _, o in UNITS[:u + 1]) for u in range(NU)]
    mm_upto = [sum(o != TRN for _, o in UNITS[:u + 1]) for u in range(NU)]
    NV, NG, NM = vec_upto[-1], gps_upto[-1], mm_upto[-1]
    TU = UNITS.index(((), TRN))

    CHUNKS = [(0, 4), (4, 8), (8, 14), (14, F - 1)]
    NC = len(CHUNKS)
    chunk_of = {i: c for c, (lo, hi) in enumerate(CHUNKS) for i in range(lo, hi)}

    def last_unit(c):
        return max(u for u, (fields, _) in enumerate(UNITS) if any(chunk_of[i] == c for i in fields))

    x_rows = x.rearrange("(t p) f d -> t p (f d)", p=P)
    out_rows = out.rearrange("(t p) c e -> t p (c e)", p=P)
    BR = 104
    assert COLS % BR == 0
    BC = COLS // BR
    b_flat = b.rearrange("c e -> (c e)")
    parts_dram = nc.dram_tensor("bias_parts", [3, COLS], bf16, kind="Internal").ap()

    ctx = ExitStack()
    with ctx:
        def sb(name, shape, dt):
            return ctx.enter_context(nc.sbuf_tensor(name, shape, dt))

        def sem(name):
            return ctx.enter_context(nc.semaphore(name))

        x_sb = [sb(f"x_sb{h}", [P, F * D], fp32) for h in range(2)]
        xT = [sb(f"xT{h}", [P, XG * P], fp32) for h in range(2)]
        out_sb = [sb(f"out_sb{h}", [P, COLS], fp32) for h in range(2)]
        t_sb = [sb(f"t_sb{n}", [P, 2 * BANK], fp32) for n in range(2)]
        W_sb = sb("W_sb", [P, W_BLOCKS * D], fp32)
        W_raw = sb("W_raw", [P, W_BLOCKS * D], fp32)
        bias_rows = sb("bias_rows", [P, COLS], bf16)
        ones = sb("ones", [P, P], bf16)
        ident = sb("ident", [P, P], fp32)
        b_sb = sb("b_sb", [BR, BC], fp32)
        b_rest = sb("b_rest", [BR, BC], fp32)
        b_parts = sb("b_parts", [BR, 3, BC], bf16)
        slot = [ctx.enter_context(nc.psum_tensor(f"slot{s}", [P, 2 * BANK], fp32)) for s in range(SLOTS)]

        x_in = [sem(f"x_in{h}") for h in range(2)]
        w_in = sem("w_in")
        w_turned = sem("w_turned")
        b_in = sem("b_in")
        b_split = sem("b_split")
        parts_out = sem("parts_out")
        bias_in = sem("bias_in")
        ones_set = sem("ones_set")
        ident_set = sem("ident_set")
        x_turned = sem("x_turned")
        xT_ready = sem("xT_ready")
        mm_done = sem("mm_done")
        vec_done = sem("vec_done")
        act_done = sem("act_done")
        gps_done = sem("gps_done")
        stored = [[sem(f"stored{h}_{c}") for c in range(NC)] for h in range(2)]

        block = ctx.enter_context(nc.Block())

        def later(n):
            return not isinstance(n, int) or n > 0

        def over_tiles(eng, tile_steps):
            for h in range(2):
                tile_steps(h, 0, h, True)
            with eng.Fori(1, TILES // 2 - 1) as k:
                for h in range(2):
                    tile_steps(k * 2 + h, k, h, True)
            for h in range(2):
                tile_steps(TILES - 2 + h, TILES // 2 - 1, h, h == 0)

        @block.sync
        def _(sp):
            sp.dma_start(b_sb[:, :], b_flat.rearrange("(r c) -> r c", r=BR)).then_inc(b_in, 16)
            for h in range(2):
                sp.dma_start(x_sb[h][:, :], x_rows[h, :, :]).then_inc(x_in[h], 16)
            sp.wait_ge(b_split, 4)
            sp.dma_start(parts_dram.rearrange("k (r c) -> r k c", r=BR), b_parts[:, :, :]).then_inc(parts_out, 16)
            sp.wait_ge(parts_out, 16)
            for q in range(ROWG):
                sp.dma_start(bias_rows[D * q:D * q + 3, :], parts_dram[:, :]).then_inc(bias_in, 16)

            def store(k, h):
                t = 2 * k + h
                ends = [last_unit(c) for c in range(NC)]
                steps = [(t * P * COLS + first_pair[lo] * D, t * NV + vec_upto[u], t * NG + gps_upto[u])
                         for (lo, _), u in zip(CHUNKS, ends)]
                if not isinstance(k, int):
                    for at, vec, gps in steps:
                        for value in (at * 4, vec, gps):
                            sp.compute_val(value)
                for c, (lo, hi) in enumerate(CHUNKS):
                    a, z = first_pair[lo] * D, first_pair[hi] * D
                    at, vec, gps = steps[c]
                    sp.wait_ge(vec_done, vec)
                    sp.wait_ge(gps_done, gps)
                    sp.dma_start(bass.AP(out.tensor, at, [[COLS, P], [1, z - a]]),
                                 out_sb[h][:, a:z]).then_inc(stored[h][c], 16)

            def next_load(t, h):
                sp.dma_start(x_sb[h][:, :], x_rows[t + 2, :, :]).then_inc(x_in[h], 16)

            for h in range(2):
                store(0, h)
                next_load(h, h)
            with sp.Fori(1, TILES // 2 - 1) as k:
                for h in range(2):
                    store(k, h)
                    next_load(k * 2 + h, h)
            for h in range(2):
                store(TILES // 2 - 1, h)
            for h in range(2):
                for c in range(NC):
                    sp.wait_ge(stored[h][c], 16 * (TILES // 2))

        @block.gpsimd
        def _(pool):
            nc.gpsimd.memset(ident[:, :], 0.0).then_inc(ident_set, 1)
            pool.wait_ge(ident_set, 1)
            nc.gpsimd.affine_select(out=ident[:, :], in_=ident[:, :], compare_op=ALU.not_equal, fill=1.0,
                                    base=0, pattern=[[-1, P]], channel_multiplier=1).then_inc(ident_set, 1)

            def tile_steps(t, k, h, more):
                pool.wait_ge(x_in[h], k * 16 + 16)
                if later(k):
                    for c in range(NC):
                        pool.wait_ge(stored[h][c], k * 16)
                for u, (fields, owner) in enumerate(UNITS):
                    if owner != GPS:
                        continue
                    n = gps_upto[u] - 1
                    pool.wait_ge(act_done, t * NG + gps_upto[u])
                    at = 0
                    for i in fields:
                        w = npairs(i) * D
                        a = first_pair[i] * D
                        last = nc.gpsimd.tensor_tensor(out_sb[h][:, a:a + w], t_sb[(h * NG + n) % 2][:, at:at + w],
                                                       x_sb[h][:, (i + 1) * D:F * D], ALU.mult)
                        at += w
                    last.then_inc(gps_done, 1)

            over_tiles(pool, tile_steps)

        @block.scalar
        def _(act):
            for i in range(F - 1):
                q, a, n = row_group[i], w_first[i] * D, npairs(i)
                p0 = first_pair[i]
                act.dma_start(W_raw[D * q:D * q + D, a:a + n * D].rearrange("e (c d) -> e c d", d=D),
                              W[p0:p0 + n, :, :].rearrange("c e d -> e c d")).then_inc(w_in, 16)

            def turn_out(h, tile):
                act.wait_ge(x_turned, tile + 1)
                nc.scalar.activation(xT[h][:, :], slot[TU % SLOTS][:, 0:XG * P], ACT.Copy).then_inc(xT_ready, 1)

            turn_out(0, 0)

            def tile_steps(t, k, h, more):
                for u, (fields, owner) in enumerate(UNITS):
                    if owner == TRN and more:
                        turn_out(1 - h, t + 1)
                    if owner == GPS:
                        n = gps_upto[u] - 1
                        w = sum(npairs(i) for i in fields) * D
                        act.wait_ge(mm_done, t * NM + mm_upto[u])
                        if later(t) or n >= 2:
                            act.wait_ge(gps_done, t * NG + n - 1)
                        nc.scalar.activation(t_sb[(h * NG + n) % 2][:, 0:w], slot[u % SLOTS][:, 0:w],
                                             ACT.Copy).then_inc(act_done, 1)

            over_tiles(act, tile_steps)

        @block.vector
        def _(dve):
            nc.vector.memset(ones[:, :], 1.0).then_inc(ones_set, 1)
            dve.wait_ge(b_in, 16)
            nc.vector.tensor_copy(b_parts[:, 0, :], b_sb[:, :]).then_inc(b_split, 1)
            dve.wait_ge(b_split, 1)
            nc.vector.tensor_tensor(b_rest[:, :], b_sb[:, :], b_parts[:, 0, :], ALU.subtract).then_inc(b_split, 1)
            dve.wait_ge(b_split, 2)
            nc.vector.tensor_copy(b_parts[:, 1, :], b_rest[:, :]).then_inc(b_split, 1)
            dve.wait_ge(b_split, 3)
            nc.vector.tensor_tensor(b_parts[:, 2, :], b_rest[:, :], b_parts[:, 1, :], ALU.subtract).then_inc(b_split, 1)
            dve.wait_ge(w_in, 16 * (F - 1))
            for q in range(ROWG):
                n = max(w_first[i] + npairs(i) for i in range(F - 1) if row_group[i] == q) * D
                rows = slice(D * q, D * q + D)
                nc.vector.transpose(W_sb[rows, 0:n], W_raw[rows, 0:n]).then_inc(w_turned, 1)

            def tile_steps(t, k, h, more):
                dve.wait_ge(x_in[h], k * 16 + 16)
                free = set()
                for u, (fields, owner) in enumerate(UNITS):
                    if owner != VEC:
                        continue
                    dve.wait_ge(mm_done, t * NM + mm_upto[u])
                    at = 0
                    for i in fields:
                        if later(k) and chunk_of[i] not in free:
                            free.add(chunk_of[i])
                            dve.wait_ge(stored[h][chunk_of[i]], k * 16)
                        w = npairs(i) * D
                        a = first_pair[i] * D
                        last = nc.vector.tensor_tensor(out_sb[h][:, a:a + w], slot[u % SLOTS][:, at:at + w],
                                                       x_sb[h][:, (i + 1) * D:F * D], ALU.mult)
                        at += w
                    last.then_inc(vec_done, 1)

            over_tiles(dve, tile_steps)

        @block.tensor
        def _(pe):
            def turn_x(s, h):
                for g in range(XG):
                    last = nc.tensor.transpose(slot[s][:, g * P:(g + 1) * P], x_sb[h][:, x_col[g]:x_col[g] + P],
                                               ident[:, :])
                last.then_inc(x_turned, 1)

            pe.wait_ge(ident_set, 2)
            pe.wait_ge(x_in[0], 16)
            turn_x(TU % SLOTS, 0)
            pe.wait_ge(ones_set, 1)
            pe.wait_ge(w_turned, ROWG)
            pe.wait_ge(bias_in, 16 * ROWG)

            def tile_steps(t, k, h, more):
                pe.wait_ge(xT_ready, t + 1)
                for u, (fields, owner) in enumerate(UNITS):
                    v = (u - SLOTS) % NU
                    tv = t if u >= SLOTS else t - 1
                    if u >= SLOTS or later(t):
                        if UNITS[v][1] == VEC:
                            pe.wait_ge(vec_done, tv * NV + vec_upto[v])
                        elif UNITS[v][1] == GPS:
                            pe.wait_ge(act_done, tv * NG + gps_upto[v])
                        elif more:
                            pe.wait_ge(xT_ready, tv + 2)
                    if owner == TRN:
                        if more:
                            pe.wait_ge(x_in[1 - h], k * 16 + 16 + 16 * h)
                            turn_x(u % SLOTS, 1 - h)
                        continue
                    at = 0
                    for i in fields:
                        q = row_group[i]
                        rows = slice(D * q, D * q + D)
                        bias = slice(D * q, D * q + 3)
                        done = 0
                        w = npairs(i) * D
                        while done < w:
                            m = min(w - done, BANK - at % BANK)
                            ps = slot[u % SLOTS][:, at:at + m]
                            a = first_pair[i] * D + done
                            nc.tensor.matmul(ps, ones[bias, :], bias_rows[bias, a:a + m], start=True, stop=False)
                            a = w_first[i] * D + done
                            g = i // ROWG
                            last = nc.tensor.matmul(ps, xT[h][rows, g * P:(g + 1) * P], W_sb[rows, a:a + m],
                                                    start=False, stop=True)
                            done += m
                            at += m
                    last.then_inc(mm_done, 1)

            over_tiles(pe, tile_steps)


_INS = ['r_x', 'L0_rec_W', 'L0_rec_b']


def kernel(**inputs):
    import numpy as _np
    import concourse.bacc as _bacc
    from concourse import mybir as _mybir
    from concourse.bass_utils import run_bass_kernel_spmd as _run

    nc = _bacc.Bacc("TRN2", target_bir_lowering=False, num_devices=1)
    arrays, args = {}, []
    for name in _INS:
        a = _np.ascontiguousarray(inputs[name])
        arrays[f"in_{name}_dram"] = a
        args.append(nc.dram_tensor(f"in_{name}_dram", a.shape, _mybir.dt.from_np(a.dtype), kind="ExternalInput").ap())
    batch, _, dim = inputs['r_x'].shape
    shape = (batch, inputs['L0_rec_W'].shape[0], dim)
    out = nc.dram_tensor("out_0_dram", shape, _mybir.dt.float32, kind="ExternalOutput").ap()
    pairwise_bilinear_kernel(nc, *args, out)
    r = _run(nc, [arrays], core_ids=[0])
    return r.results[0]["out_0_dram"]
```

```python
import concourse.bass as bass
from concourse import mybir
from contextlib import ExitStack


def pairwise_bilinear_kernel(nc: bass.Bass, x: bass.AP, W: bass.AP, b: bass.AP, out: bass.AP):
    fp32 = mybir.dt.float32
    fp32r = mybir.dt.float32r
    bf16 = mybir.dt.bfloat16
    ALU = mybir.AluOpType
    ACT = mybir.ActivationFunctionType

    P = 128
    BATCH, F, D = x.shape
    PAIRS = F * (F - 1) // 2
    TILES = BATCH // P
    COLS = PAIRS * D
    BANK = 512
    SLOTS = 4
    PARTS = P // D

    def pairs_of(lo, hi):
        return sum(F - 1 - i for i in range(lo, hi))

    first_pair = [pairs_of(0, i) for i in range(F)]

    VEC, GPS = "v", "g"
    UNITS = [(0, 1, VEC), (1, 2, VEC), (2, 3, VEC), (3, 4, GPS), (4, 5, VEC), (5, 6, VEC), (6, 7, VEC),
             (7, 8, GPS), (8, 9, VEC), (9, 10, VEC), (10, 12, VEC), (12, 14, VEC), (14, 16, GPS),
             (16, 18, VEC), (18, 21, GPS), (21, F - 1, GPS)]
    assert all(pairs_of(lo, hi) * D <= 2 * BANK for lo, hi, _ in UNITS)
    NG = sum(o == GPS for _, _, o in UNITS)
    gps_upto = [sum(o == GPS for _, _, o in UNITS[:u + 1]) for u in range(len(UNITS))]
    T_COLS = max(pairs_of(lo, hi) * D for lo, hi, o in UNITS if o == GPS)

    PIECES = [(0, 7), (7, 13), (13, 19), (19, F - 1)]
    assert all((hi - lo) * P <= 2 * BANK for lo, hi in PIECES)
    W_CHUNKS = [(0, 4), (4, 10), (10, F - 1)]
    assert all(pairs_of(lo, hi) <= P for lo, hi in W_CHUNKS)
    EG = 2 * BANK // P
    W_STEPS = D // EG
    CHUNKS = [(0, 2), (2, 4), (4, 8), (8, 14), (14, 18), (18, F - 1)]
    NC = len(CHUNKS)
    chunk_of = {i: c for c, (lo, hi) in enumerate(CHUNKS) for i in range(lo, hi)}

    AHEAD = 3
    LOAD_AT = 1

    def items(text):
        return [(w[0], int(w[1:])) if w != "-" else None for w in text.split()]

    FIRST = items("X0 W0 W1 W2 W3 M0 M1 W4 M2 W5 M3 W6 W7 X1 M4 M5 W8 M6 W9 M7 W10 M8 W11 X2 "
                  "M9 X3 M10 T0 M11 M12 T1 M13 T2 M14 T3 M15")
    REST = items("M0 M1 M2 M3 M4 M5 M6 M7 M8 T0 M9 M10 T1 M11 M12 T2 M13 M14 T3 M15")
    LAST = [item if item[0] == "M" else None for item in REST]
    assert len(FIRST) % SLOTS == 0 and len(REST) % SLOTS == 0

    def by_vec(item):
        return item is not None and (UNITS[item[1]][2] == VEC if item[0] == "M" else item[0] == "W" and item[1] % 2 == 0)

    def by_act(item):
        return item is not None and not by_vec(item)

    def is_split(item):
        return item is not None and item[0] != "M"

    def is_item(item):
        return item is not None

    def same(n, value):
        return isinstance(n, int) and n == value

    def list_of(t):
        return FIRST if same(t, 0) else (LAST if same(t, TILES - 1) else REST)

    def before(t, kind):
        return 0 if same(t, 0) else sum(map(kind, FIRST)) + (t - 1) * sum(map(kind, REST))

    def upto(t, kind, n):
        if n < 0:
            prev = FIRST if same(t, 1) else REST
            return before(t, kind) - sum(map(kind, prev[len(prev) + n + 1:]))
        return before(t, kind) + sum(map(kind, list_of(t)[:n + 1]))

    x_rows = x.rearrange("(t p) f d -> t p (f d)", p=P)
    BR = 104
    assert COLS % BR == 0
    parts_dram = nc.dram_tensor("bias_parts", [3, COLS], bf16, kind="Internal").ap()

    ctx = ExitStack()
    with ctx:
        def sb(name, shape, dt):
            return ctx.enter_context(nc.sbuf_tensor(name, shape, dt))

        def sem(name):
            return ctx.enter_context(nc.semaphore(name))

        x_sb = [sb(f"x_sb{h}", [P, F, D], fp32) for h in range(2)]
        x_parts = sb("x_parts", [P, F - 1, PARTS, D], fp32r)
        x_stack = [sb(f"x_stack{h}", [P, (F - 1) * P], fp32r) for h in range(2)]
        W_parts = [sb(f"W_parts{n}", [P, EG, PARTS, D], fp32r) for n in range(2)]
        W_stack = sb("W_stack", [P, COLS], fp32r)
        bias_rows = sb("bias_rows", [P, COLS], bf16)
        out_sb = [sb(f"out_sb{h}", [P, COLS], fp32) for h in range(2)]
        t_sb = [sb(f"t_sb{n}", [P, T_COLS], fp32) for n in range(2)]
        ones = sb("ones", [P, P], bf16)
        ident = sb("ident", [P, P], fp32)
        ident_r = sb("ident_r", [P, P], fp32r)
        b_sb = sb("b_sb", [BR, COLS // BR], fp32)
        b_rest = sb("b_rest", [BR, COLS // BR], fp32)
        b_parts = sb("b_parts", [BR, 3, COLS // BR], bf16)
        slot = [ctx.enter_context(nc.psum_tensor(f"slot{s}", [P, 2 * BANK], fp32)) for s in range(SLOTS)]

        W_raw = [out_sb[1][:, c * D * D:(c + 1) * D * D].rearrange("p (e d) -> p e d", d=D)
                 for c in range(len(W_CHUNKS))]

        x_in = [sem(f"x_in{h}") for h in range(2)]
        w_in = [sem(f"w_in{c}") for c in range(len(W_CHUNKS))]
        b_in = sem("b_in")
        b_split = sem("b_split")
        parts_out = sem("parts_out")
        bias_zero = sem("bias_zero")
        bias_in = sem("bias_in")
        ones_set = sem("ones_set")
        ident_set = sem("ident_set")
        high_done = sem("high_done")
        low_done = sem("low_done")
        filled = sem("filled")
        vec_done = sem("vec_done")
        act_done = sem("act_done")
        gps_done = sem("gps_done")
        stored = [[sem(f"stored{h}_{c}") for c in range(NC)] for h in range(2)]

        block = ctx.enter_context(nc.Block())

        def over_tiles(eng, tile_steps):
            for h in range(2):
                tile_steps(h, 0, h)
            with eng.Fori(1, TILES // 2 - 1) as k:
                for h in range(2):
                    tile_steps(k * 2 + h, k, h)
            for h in range(2):
                tile_steps(TILES - 2 + h, TILES // 2 - 1, h)

        def split_views(item, h):
            kind, n = item
            if kind == "W":
                c, g = divmod(n, W_STEPS)
                np = pairs_of(*W_CHUNKS[c])
                src = W_raw[c][0:np, g * EG:(g + 1) * EG, :]
                parts = W_parts[n % 2][0:np, :, :, :]
                high, low = parts[:, :, 0::2, :], parts[:, :, 1::2, :]
            else:
                lo, hi = PIECES[n]
                src = x_sb[h if kind == "X" else 1 - h][:, lo:hi, :]
                parts = x_parts[:, lo:hi, :, :]
                high, low = parts[:, :, 0:2, :], parts[:, :, 2:4, :]
            rows, m, _ = src.shape
            return src.unsqueeze(2).to_broadcast([rows, m, 2, D]), high, low

        def empty_views(item, s, h):
            kind, n = item
            if kind == "W":
                c, g = divmod(n, W_STEPS)
                p0, np = first_pair[W_CHUNKS[c][0]], pairs_of(*W_CHUNKS[c])
                src = slot[s][:, :].rearrange("k (e p) -> k p e", p=P)[:, 0:np, :]
                dst = W_stack[:, p0 * D:(p0 + np) * D].rearrange("k (p e) -> k p e", e=D)
                return src, dst[:, :, g * EG:(g + 1) * EG]
            lo, hi = PIECES[n]
            return slot[s][:, 0:(hi - lo) * P], x_stack[h if kind == "X" else 1 - h][:, lo * P:hi * P]

        @block.sync
        def _(sp):
            sp.dma_start(x_sb[0][:, :, :].rearrange("p f d -> p (f d)"), x_rows[0, :, :]).then_inc(x_in[0], 16)
            for c, (lo, hi) in enumerate(W_CHUNKS):
                np = pairs_of(lo, hi)
                sp.dma_start(W_raw[c][0:np, :, :], W[first_pair[lo]:first_pair[lo] + np, :, :]).then_inc(w_in[c], 16)
            sp.dma_start(x_sb[1][:, :, :].rearrange("p f d -> p (f d)"), x_rows[1, :, :]).then_inc(x_in[1], 16)

            sp.wait_ge(b_split, 4)
            sp.dma_start(parts_dram.rearrange("k (r c) -> r k c", r=BR), b_parts[:, :, :]).then_inc(parts_out, 16)
            sp.wait_ge(parts_out, 16)
            sp.wait_ge(bias_zero, 1)
            sp.dma_start(bias_rows[0:3, :], parts_dram[:, :]).then_inc(bias_in, 16)

            def store(t, k, h):
                steps = []
                for lo, hi in CHUNKS:
                    units = [u for u, (a, _, _) in enumerate(UNITS) if lo <= a < hi]
                    n = list_of(t).index(("M", units[-1]))
                    steps.append((t * P * COLS + first_pair[lo] * D, upto(t, by_vec, n), t * NG + gps_upto[units[-1]]))
                if not isinstance(t, int):
                    for at, vec, gps in steps:
                        for value in (at * 4, vec, gps):
                            sp.compute_val(value)
                for c, (lo, hi) in enumerate(CHUNKS):
                    at, vec, gps = steps[c]
                    a, z = first_pair[lo] * D, first_pair[hi] * D
                    sp.wait_ge(vec_done, vec)
                    if not same(gps, 0):
                        sp.wait_ge(gps_done, gps)
                    sp.dma_start(bass.AP(out.tensor, at, [[COLS, P], [1, z - a]]),
                                 out_sb[h][:, a:z]).then_inc(stored[h][c], 16)

            over_tiles(sp, store)
            for h in range(2):
                for c in range(NC):
                    sp.wait_ge(stored[h][c], 16 * (TILES // 2))

        @block.gpsimd
        def _(pool):
            nc.gpsimd.memset(ident[:, :], 0.0).then_inc(ident_set, 1)
            pool.wait_ge(ident_set, 1)
            nc.gpsimd.affine_select(out=ident[:, :], in_=ident[:, :], compare_op=ALU.not_equal, fill=1.0,
                                    base=0, pattern=[[-1, P]], channel_multiplier=1).then_inc(ident_set, 1)
            nc.gpsimd.memset(bias_rows[:, :].bitcast(fp32), 0.0).then_inc(bias_zero, 1)
            nc.gpsimd.memset(ones[:, :], 0.0).then_inc(ones_set, 1)
            pool.wait_ge(ones_set, 1)
            nc.gpsimd.memset(ones[0:3, :], 1.0).then_inc(ones_set, 1)

            def tile_steps(t, k, h):
                pool.wait_ge(x_in[h], k * 16 + 16)
                freed = set()
                for n, item in enumerate(list_of(t)):
                    if item is None or item[0] != "M" or UNITS[item[1]][2] != GPS:
                        continue
                    lo, hi, _ = UNITS[item[1]]
                    g = gps_upto[item[1]] - 1
                    pool.wait_ge(act_done, upto(t, by_act, n))
                    at = 0
                    for i in range(lo, hi):
                        if not same(k, 0) and chunk_of[i] not in freed:
                            freed.add(chunk_of[i])
                            pool.wait_ge(stored[h][chunk_of[i]], k * 16)
                        w = pairs_of(i, i + 1) * D
                        a = first_pair[i] * D
                        last = nc.gpsimd.tensor_tensor(
                            out_sb[h][:, a:a + w], t_sb[(h * NG + g) % 2][:, at:at + w],
                            x_sb[h][:, i + 1:F, :].rearrange("p f d -> p (f d)"), ALU.mult)
                        at += w
                    last.then_inc(gps_done, 1)

            over_tiles(pool, tile_steps)

        @block.scalar
        def _(act):
            act.dma_start(b_sb[:, :], b.rearrange("c e -> (c e)").rearrange("(r c) -> r c", r=BR)).then_inc(b_in, 16)

            def high_parts(t, k, h, n):
                item = list_of(t)[n]
                kind, m = item
                if kind == "W":
                    c, g = divmod(m, W_STEPS)
                    if g == 0:
                        act.wait_ge(w_in[c], 16)
                    if m >= 2:
                        act.wait_ge(filled, upto(t, is_item, FIRST.index(("W", m - 2))))
                elif kind == "X":
                    if m == 0:
                        act.wait_ge(x_in[h], 16)
                else:
                    if m == 0:
                        act.wait_ge(x_in[1 - h], k * 16 + 16 + 16 * h)
                        if not same(t, 0):
                            act.wait_ge(filled, before(t, is_item))
                    if same(t, 0):
                        act.wait_ge(filled, upto(t, is_item, FIRST.index(("X", m))))
                src, high, _ = split_views(item, h)
                nc.scalar.activation(high, src, ACT.Copy).then_inc(high_done, 1)

            def tile_steps(t, k, h):
                todo = list_of(t)
                if same(t, 0):
                    for n in range(AHEAD):
                        if is_split(todo[n]):
                            high_parts(t, k, h, n)
                for n, item in enumerate(todo):
                    if n == LOAD_AT and not same(t, 0) and not same(t, TILES - 1):
                        act.wait_ge(vec_done, before(t, by_vec))
                        act.wait_ge(gps_done, t * NG)
                        act.dma_start(x_sb[1 - h][:, :, :].rearrange("p f d -> p (f d)"),
                                      x_rows[t + 1, :, :]).then_inc(x_in[1 - h], 16)
                    if n + AHEAD < len(todo) and is_split(todo[n + AHEAD]):
                        high_parts(t, k, h, n + AHEAD)
                    if not by_act(item):
                        continue
                    s = n % SLOTS
                    act.wait_ge(filled, upto(t, is_item, n))
                    if item[0] != "M":
                        src, dst = empty_views(item, s, h)
                    else:
                        lo, hi, _ = UNITS[item[1]]
                        g = gps_upto[item[1]] - 1
                        if not same(t, 0) or g >= 2:
                            act.wait_ge(gps_done, t * NG + g - 1)
                        w = pairs_of(lo, hi) * D
                        src, dst = slot[s][:, 0:w], t_sb[(h * NG + g) % 2][:, 0:w]
                    nc.scalar.activation(dst, src, ACT.Copy).then_inc(act_done, 1)

            over_tiles(act, tile_steps)

        @block.vector
        def _(dve):
            dve.wait_ge(ident_set, 2)
            nc.vector.tensor_copy(ident_r[:, :], ident[:, :]).then_inc(ident_set, 1)

            def split_bias():
                dve.wait_ge(b_in, 16)
                nc.vector.tensor_copy(b_parts[:, 0, :], b_sb[:, :]).then_inc(b_split, 1)
                dve.wait_ge(b_split, 1)
                nc.vector.tensor_tensor(b_rest[:, :], b_sb[:, :], b_parts[:, 0, :], ALU.subtract).then_inc(b_split, 1)
                dve.wait_ge(b_split, 2)
                nc.vector.tensor_copy(b_parts[:, 1, :], b_rest[:, :]).then_inc(b_split, 1)
                dve.wait_ge(b_split, 3)
                nc.vector.tensor_tensor(b_parts[:, 2, :], b_rest[:, :], b_parts[:, 1, :], ALU.subtract)\
                    .then_inc(b_split, 1)

            def low_parts(t, k, h, n):
                item = list_of(t)[n]
                dve.wait_ge(high_done, upto(t, is_split, n))
                src, high, low = split_views(item, h)
                nc.vector.tensor_tensor(low, src, high.bitcast(fp32), ALU.subtract).then_inc(low_done, 1)

            def tile_steps(t, k, h):
                todo = list_of(t)
                if same(t, 0):
                    for n in range(AHEAD - 1):
                        if is_split(todo[n]):
                            low_parts(t, k, h, n)
                        if n == 0:
                            split_bias()
                dve.wait_ge(x_in[h], k * 16 + 16)
                freed = set()
                for n, item in enumerate(todo):
                    if n + AHEAD - 1 < len(todo) and is_split(todo[n + AHEAD - 1]):
                        low_parts(t, k, h, n + AHEAD - 1)
                    if not by_vec(item):
                        continue
                    s = n % SLOTS
                    dve.wait_ge(filled, upto(t, is_item, n))
                    if item[0] != "M":
                        src, dst = empty_views(item, s, h)
                        nc.vector.tensor_copy(dst, src).then_inc(vec_done, 1)
                        continue
                    lo, hi, _ = UNITS[item[1]]
                    at = 0
                    for i in range(lo, hi):
                        if not same(k, 0) and chunk_of[i] not in freed:
                            freed.add(chunk_of[i])
                            dve.wait_ge(stored[h][chunk_of[i]], k * 16)
                        w = pairs_of(i, i + 1) * D
                        a = first_pair[i] * D
                        last = nc.vector.tensor_tensor(
                            out_sb[h][:, a:a + w], slot[s][:, at:at + w],
                            x_sb[h][:, i + 1:F, :].rearrange("p f d -> p (f d)"), ALU.mult)
                        at += w
                    last.then_inc(vec_done, 1)

            over_tiles(dve, tile_steps)

        @block.tensor
        def _(pe):
            pe.wait_ge(ident_set, 3)

            def slot_free(t, n):
                v = n - SLOTS
                while v >= 0 and list_of(t)[v] is None:
                    v -= SLOTS
                if v < 0 and same(t, 0):
                    return
                prev = list_of(t)[v] if v >= 0 else (FIRST if same(t, 1) else REST)[v]
                if by_vec(prev):
                    pe.wait_ge(vec_done, upto(t, by_vec, v))
                else:
                    pe.wait_ge(act_done, upto(t, by_act, v))

            def turn(item, s, h):
                kind, m = item
                if kind == "W":
                    np = pairs_of(*W_CHUNKS[m // W_STEPS])
                    blocks = [W_parts[m % 2][0:np, e, :, :] for e in range(EG)]
                else:
                    blocks = [x_parts[:, i, :, :] for i in range(*PIECES[m])]
                for n, parts in enumerate(blocks):
                    parts = parts.rearrange("p r d -> p (r d)")
                    last = nc.tensor.matmul(slot[s][:, n * P:(n + 1) * P], parts, ident_r[0:parts.shape[0], :],
                                            start=True, stop=True)
                last.then_inc(filled, 1)

            def products(u, s, h):
                lo, hi, _ = UNITS[u]
                a0, w = first_pair[lo] * D, pairs_of(lo, hi) * D
                for bank in range(0, w, BANK):
                    end = min(bank + BANK, w)
                    nc.tensor.matmul(slot[s][:, bank:end], ones[:, :], bias_rows[:, a0 + bank:a0 + end],
                                     start=True, stop=False)
                    for i in range(lo, hi):
                        a = max(first_pair[i] * D - a0, bank)
                        z = min(first_pair[i + 1] * D - a0, end)
                        if a < z:
                            last = nc.tensor.matmul(slot[s][:, a:z], x_stack[h][:, i * P:(i + 1) * P],
                                                    W_stack[:, a0 + a:a0 + z], start=False, stop=(z == end))
                last.then_inc(filled, 1)

            def tile_steps(t, k, h):
                todo = list_of(t)
                turned = set()
                for n, item in enumerate(todo):
                    if item is None:
                        continue
                    slot_free(t, n)
                    if item[0] != "M":
                        pe.wait_ge(low_done, upto(t, is_split, n))
                        turn(item, n % SLOTS, h)
                        continue
                    lo, hi, _ = UNITS[item[1]]
                    for p, (a, z) in enumerate(PIECES):
                        if a < hi and lo < z and p not in turned:
                            turned.add(p)
                            if same(t, 0):
                                pe.wait_ge(act_done, upto(0, by_act, FIRST.index(("X", p))))
                            else:
                                prev = FIRST if same(t, 1) else REST
                                pe.wait_ge(act_done, upto(t, by_act, prev.index(("T", p)) - len(prev)))
                    if same(t, 0):
                        for c, (a, z) in enumerate(W_CHUNKS):
                            if lo == a:
                                done = FIRST.index(("W", (c + 1) * W_STEPS - 1))
                                pe.wait_ge(vec_done, upto(0, by_vec, done))
                                pe.wait_ge(act_done, upto(0, by_act, done))
                        if item[1] == 0:
                            pe.wait_ge(ones_set, 2)
                            pe.wait_ge(bias_in, 16)
                    products(item[1], n % SLOTS, h)

            over_tiles(pe, tile_steps)


_INS = ['r_x', 'L0_rec_W', 'L0_rec_b']


def kernel(**inputs):
    import numpy as _np
    import concourse.bacc as _bacc
    from concourse import mybir as _mybir
    from concourse.bass_utils import run_bass_kernel_spmd as _run

    nc = _bacc.Bacc("TRN2", target_bir_lowering=False, num_devices=1)
    arrays, args = {}, []
    for name in _INS:
        a = _np.ascontiguousarray(inputs[name])
        arrays[f"in_{name}_dram"] = a
        args.append(nc.dram_tensor(f"in_{name}_dram", a.shape, _mybir.dt.from_np(a.dtype), kind="ExternalInput").ap())
    batch, _, dim = inputs['r_x'].shape
    shape = (batch, inputs['L0_rec_W'].shape[0], dim)
    out = nc.dram_tensor("out_0_dram", shape, _mybir.dt.float32, kind="ExternalOutput").ap()
    pairwise_bilinear_kernel(nc, *args, out)
    r = _run(nc, [arrays], core_ids=[0])
    return r.results[0]["out_0_dram"]
```

```python
import concourse.bass as bass
from concourse import mybir
from contextlib import ExitStack


def pairwise_bilinear_kernel(nc: bass.Bass, x: bass.AP, W: bass.AP, b: bass.AP, out: bass.AP):
    fp32 = mybir.dt.float32
    fp32r = mybir.dt.float32r
    bf16 = mybir.dt.bfloat16
    ALU = mybir.AluOpType
    ACT = mybir.ActivationFunctionType

    P = 128
    BATCH, F, D = x.shape
    PAIRS = F * (F - 1) // 2
    TILES = BATCH // P
    COLS = PAIRS * D
    BANK = 512
    SLOTS = 4
    PARTS = P // D

    def pairs_of(lo, hi):
        return sum(F - 1 - i for i in range(lo, hi))

    first_pair = [pairs_of(0, i) for i in range(F)]

    VEC, GPS = "v", "g"
    UNITS = [(0, 1, VEC), (1, 2, VEC), (2, 3, VEC), (3, 4, GPS), (4, 5, VEC), (5, 6, VEC), (6, 7, VEC),
             (7, 8, GPS), (8, 9, VEC), (9, 10, VEC), (10, 12, VEC), (12, 14, VEC), (14, 16, GPS),
             (16, 18, VEC), (18, 21, GPS), (21, F - 1, GPS)]
    assert all(pairs_of(lo, hi) * D <= 2 * BANK for lo, hi, _ in UNITS)

    PIECES = [(0, 7), (7, 13), (13, 19), (19, F - 1)]
    assert all((hi - lo) * P <= 2 * BANK for lo, hi in PIECES)
    EG = 2 * BANK // P
    W_PAIRS = P * EG // D
    W_STEPS = -(-PAIRS // W_PAIRS)
    W_LOADS = [(0, 1), (1, 3), (3, 6), (6, W_STEPS - 1), (W_STEPS - 1, W_STEPS)]

    def w_rows(m):
        return min(P, (PAIRS - m * W_PAIRS) * D // EG)

    CHUNKS = [(0, 2), (2, 4), (4, 8), (8, 14), (14, 18), (18, F - 1)]
    FIRST_CHUNKS = [(0, 1), (1, 2), (2, 3), (3, 4), (4, 6), (6, 8), (8, 10), (10, 14), (14, 18), (18, F - 1)]
    NC = len(CHUNKS)
    chunk_of = {i: c for c, (lo, hi) in enumerate(CHUNKS) for i in range(lo, hi)}
    extra = [sum(lo <= a < hi for a, _ in FIRST_CHUNKS) - 1 for lo, hi in CHUNKS]

    WARM_UP = 10
    AHEAD = 4
    W_HIGH_AHEAD, W_LOW_AHEAD = 9, 7
    COPY_AT = 5

    def items(text):
        result = []
        for word in text.split():
            name = word.rstrip("vga").rstrip("'")
            if name == "-":
                result.append(None)
                continue
            n = int(name[1:])
            usual = {"M": UNITS[n % len(UNITS)][2], "W": VEC if n % 2 == 0 else "a"}.get(name[0], "a")
            result.append((name[0], n, -1 if "'" in word else 0, word[-1] if word[-1] in "vga" else usual))
        return result

    def find(todo, kind, n, off=0):
        return next(i for i, item in enumerate(todo) if item is not None and item[:3] == (kind, n, off))

    REST = items("M0 M1 M2 M3 M4 M5 M6 M7 M8 T0 M9 M10 T1 M11 M12 T2 M13 M14 T3 M15")
    TAIL = len(REST) - find(REST, "T", 0)
    FIRST = items("- W0 X0' W1 W2 X1' M0'g M1' M2' X0 W3 W4 M0 M3' M4' W5 M5'g W6a M6' M1 W7 M7' W8 "
                  "X2' M8' M2 M9' M3 W9 M10' M4g X1 M11' M5g X3' W10 M6 X2 M7 M12' M13' X3 M14' M8 M15'v") + REST[-TAIL:]
    FIRST_COPY_AT = find(FIRST, "T", len(PIECES) - 1)
    LAST = [item if item[0] == "M" else None for item in REST]
    assert len(FIRST) % SLOTS == 0 and len(REST) % SLOTS == 0

    def by_vec(item):
        return item is not None and item[3] == VEC

    def by_act(item):
        return item is not None and item[3] != VEC

    def by_gps(item):
        return item is not None and item[3] == GPS

    T_COLS = max(pairs_of(*UNITS[item[1]][:2]) * D for item in FIRST + REST if by_gps(item))

    def is_x(item):
        return item is not None and item[0] in "XT"

    def is_w(item):
        return item is not None and item[0] == "W"

    def is_item(item):
        return item is not None

    def low_by_vec(m):
        return m in (0, 2, 3, 4, 5, 6)

    def same(n, value):
        return isinstance(n, int) and n == value

    def list_of(t):
        return FIRST if same(t, 1) else (LAST if same(t, TILES - 1) else REST)

    def before(t, kind):
        return 0 if same(t, 1) else sum(map(kind, FIRST)) + (t - 2) * sum(map(kind, REST))

    def upto(t, kind, n):
        if n < 0:
            return before(t, kind) - sum(map(kind, REST[len(REST) + n + 1:]))
        return before(t, kind) + sum(map(kind, list_of(t)[:n + 1]))

    x_rows = x.rearrange("(t p) f d -> t p (f d)", p=P)
    BR = 104
    assert COLS % BR == 0

    ctx = ExitStack()
    with ctx:
        def sb(name, shape, dt):
            return ctx.enter_context(nc.sbuf_tensor(name, shape, dt))

        def sem(name):
            return ctx.enter_context(nc.semaphore(name))

        x_sb = [sb(f"x_sb{h}", [P, F, D], fp32) for h in range(2)]
        x_next = sb("x_next", [P, F, D], fp32)
        x_parts = sb("x_parts", [P, F - 1, PARTS, D], fp32r)
        x_stack = [sb(f"x_stack{h}", [P, (F - 1) * P], fp32r) for h in range(2)]
        W_buf = [sb(f"W_buf{n}", [P, EG * P], fp32r) for n in range(2)]
        W_stack = sb("W_stack", [P, COLS], fp32r)
        bias_rows = sb("bias_rows", [P, COLS], bf16)
        out_sb = [sb(f"out_sb{h}", [P, COLS], fp32) for h in range(2)]
        t_sb = [sb(f"t_sb{n}", [P, T_COLS], fp32) for n in range(2)]
        ones = sb("ones", [P, P], bf16)
        ident = sb("ident", [P, P], fp32)
        ident_r = sb("ident_r", [P, P], fp32r)
        b_sb = sb("b_sb", [BR, COLS // BR], fp32)
        b_rest = sb("b_rest", [BR, COLS // BR], fp32)
        b_parts = sb("b_parts", [BR, 3, COLS // BR], bf16)
        slot = [ctx.enter_context(nc.psum_tensor(f"slot{s}", [P, 2 * BANK], fp32)) for s in range(SLOTS)]

        RAW = COLS - W_STEPS * EG * D
        W_raw = out_sb[0][:, RAW:COLS].rearrange("p (s e d) -> p s e d", e=EG, d=D)

        W_BUFS = 4
        FULL = (F - 1) * P
        W_parts = [buf.rearrange("p (e r d) -> p e r d", r=PARTS, d=D)
                   for buf in (x_stack[1][:, FULL - EG * P:FULL], W_buf[0][:, :], W_buf[1][:, :],
                               x_stack[0][:, FULL - EG * P:FULL])]
        for n, off in ((0, 0), (3, -1)):
            users = [find(FIRST, "W", m) for m in range(W_STEPS) if m % W_BUFS == n]
            assert all(find(FIRST, "X", p, off) > max(users) for p, (_, hi) in enumerate(PIECES) if hi * P > FULL - EG * P)

        ZERO_AT = COLS // 2

        def t_buf(t, h, n):
            base = 0 if same(t, 1) else sum(map(by_gps, FIRST)) + h * sum(map(by_gps, REST))
            return (base + sum(map(by_gps, list_of(t)[:n]))) % 2

        def raw_read(eng):
            eng.wait_ge(w_low_vec, sum(map(low_by_vec, range(W_STEPS))))
            eng.wait_ge(w_low_gps, W_STEPS - sum(map(low_by_vec, range(W_STEPS))))

        def over_raw(item):
            return item[2] == -1 and first_pair[UNITS[item[1]][1]] * D > RAW

        x_in = [sem(f"x_in{h}") for h in range(2)]
        w_in = [sem(f"w_in{c}") for c in range(len(W_LOADS))]
        next_in = sem("next_in")
        moved = sem("moved")
        b_in = sem("b_in")
        b_split = sem("b_split")
        warm_set = sem("warm_set")
        bias_zero = sem("bias_zero")
        bias_in = sem("bias_in")
        ones_set = sem("ones_set")
        ident_set = sem("ident_set")
        high_done = sem("high_done")
        low_done = sem("low_done")
        w_high_done = sem("w_high_done")
        w_low_vec = sem("w_low_vec")
        w_low_gps = sem("w_low_gps")
        filled = sem("filled")
        vec_done = sem("vec_done")
        act_done = sem("act_done")
        gps_done = sem("gps_done")
        stored = [[sem(f"stored{h}_{c}") for c in range(NC)] for h in range(2)]

        block = ctx.enter_context(nc.Block())

        def over_stages(eng, stage):
            stage(1, 0, 1)
            with eng.Fori(1, TILES // 2 - 1) as k:
                for h in range(2):
                    stage(k * 2 + h, k, h)
            for h in range(2):
                stage(TILES - 2 + h, TILES // 2 - 1, h)

        def split_views(item, t, h):
            kind, n, off, _ = item
            if kind == "W":
                src = W_raw[0:w_rows(n), n, :, :]
                parts = W_parts[n % W_BUFS][0:w_rows(n), :, :, :]
                high, low = parts[:, :, 0::2, :], parts[:, :, 1::2, :]
            else:
                lo, hi = PIECES[n]
                x_src = x_sb[(h + off) % 2] if kind == "X" else x_next if same(t, 1) else x_sb[1 - h]
                src = x_src[:, lo:hi, :]
                parts = x_parts[:, lo:hi, :, :]
                high, low = parts[:, :, 0:2, :], parts[:, :, 2:4, :]
            rows, m, _ = src.shape
            return src.unsqueeze(2).to_broadcast([rows, m, 2, D]), high, low

        def empty_views(item, s, h):
            kind, n, off, _ = item
            if kind == "W":
                rows = w_rows(n)
                src = slot[s][:, :].rearrange("k (e p) -> k p e", p=P)[:, 0:rows, :]
                a = n * W_PAIRS * D
                return src, W_stack[:, a:a + rows * EG].rearrange("k (p e) -> k p e", e=EG)
            lo, hi = PIECES[n]
            return slot[s][:, 0:(hi - lo) * P], x_stack[(h + off) % 2 if kind == "X" else 1 - h][:, lo * P:hi * P]

        @block.sync
        def _(sp):
            def load_w(c):
                lo, hi = W_LOADS[c]
                rows = w_rows(lo)
                n = (hi - lo) * rows * EG * D
                src = W.rearrange("c e d -> (c e d)")[lo * P * EG * D:lo * P * EG * D + n]
                sp.dma_start(W_raw[0:rows, lo:hi, :, :], src.rearrange("(s p e d) -> p s e d", p=rows, e=EG, d=D))\
                    .then_inc(w_in[c], 16)

            def load_x(dst, t):
                return sp.dma_start(dst[:, :, :].rearrange("p f d -> p (f d)"), x_rows[t, :, :])

            load_w(0)
            load_x(x_sb[0], 0).then_inc(x_in[0], 16)
            for c in range(1, len(W_LOADS)):
                load_w(c)

            sp.wait_ge(bias_zero, 2)
            for part, done in enumerate((1, 3, 4)):
                sp.wait_ge(b_split, done)
                sp.dma_start(bias_rows[part:part + 1, :], b_parts[:, part, :]).then_inc(bias_in, 16)

            load_x(x_sb[1], 1).then_inc(x_in[1], 16)
            load_x(x_next, 2).then_inc(next_in, 16)

            def store(t, k, h):
                todo = list_of(t)
                steps = []
                for off in ((-1, 0) if same(t, 1) else (0,)):
                    for lo, hi in (FIRST_CHUNKS if same(t, 1) else CHUNKS):
                        n = max(find(todo, "M", u, off) for u, (a, _, _) in enumerate(UNITS) if lo <= a < hi)
                        steps.append((n, off, lo, hi, (t + off) * P * COLS + first_pair[lo] * D,
                                      upto(t, by_vec, n), upto(t, by_gps, n)))
                steps.sort(key=lambda step: step[0])
                if not isinstance(t, int):
                    for _, _, _, _, at, vec, gps in steps:
                        for value in (at * 4, vec, gps):
                            sp.compute_val(value)
                for _, off, lo, hi, at, vec, gps in steps:
                    a, z = first_pair[lo] * D, first_pair[hi] * D
                    own = (h + off) % 2
                    if not same(vec, 0):
                        sp.wait_ge(vec_done, vec)
                    if not same(gps, 0):
                        sp.wait_ge(gps_done, gps)
                    sp.dma_start(bass.AP(out.tensor, at, [[COLS, P], [1, z - a]]),
                                 out_sb[own][:, a:z]).then_inc(stored[own][chunk_of[lo]], 16)

            over_stages(sp, store)
            for h in range(2):
                for c in range(NC):
                    sp.wait_ge(stored[h][c], (TILES // 2 + extra[c]) * 16)

        @block.gpsimd
        def _(pool):
            nc.gpsimd.memset(ident[:, :], 0.0).then_inc(ident_set, 1)
            pool.wait_ge(ident_set, 1)
            nc.gpsimd.affine_select(out=ident[:, :], in_=ident[:, :], compare_op=ALU.not_equal, fill=1.0,
                                    base=0, pattern=[[-1, P]], channel_multiplier=1).then_inc(ident_set, 1)
            nc.gpsimd.memset(ones[:, :], 0.0).then_inc(ones_set, 1)
            pool.wait_ge(ones_set, 1)
            nc.gpsimd.memset(ones[0:3, :], 1.0).then_inc(ones_set, 1)
            nc.gpsimd.memset(bias_rows[:, ZERO_AT:].bitcast(fp32), 0.0).then_inc(bias_zero, 1)

            def w_low_parts(m):
                pool.wait_ge(w_high_done, m + 1)
                src, high, low = split_views(("W", m, 0, None), 1, 1)
                nc.gpsimd.tensor_tensor(low, src, high.bitcast(fp32), ALU.subtract).then_inc(w_low_gps, 1)

            def stage(t, k, h):
                todo = list_of(t)
                if same(t, 1):
                    for item in todo[:W_LOW_AHEAD]:
                        if is_w(item) and not low_by_vec(item[1]):
                            w_low_parts(item[1])
                else:
                    pool.wait_ge(moved, t - 1)
                freed, seen = set(), set()
                for n, item in enumerate(todo):
                    if same(t, 1) and n + W_LOW_AHEAD < len(todo):
                        ahead = todo[n + W_LOW_AHEAD]
                        if is_w(ahead) and not low_by_vec(ahead[1]):
                            w_low_parts(ahead[1])
                    if not by_gps(item):
                        continue
                    lo, hi, _ = UNITS[item[1]]
                    own = (h + item[2]) % 2
                    pool.wait_ge(act_done, upto(t, by_act, n))
                    if over_raw(item):
                        raw_read(pool)
                    if same(t, 1) and own not in seen:
                        seen.add(own)
                        pool.wait_ge(x_in[own], 16)
                    at = 0
                    for i in range(lo, hi):
                        if not same(k, 0) and chunk_of[i] not in freed:
                            freed.add(chunk_of[i])
                            pool.wait_ge(stored[h][chunk_of[i]], (k + extra[chunk_of[i]]) * 16)
                        w = pairs_of(i, i + 1) * D
                        a = first_pair[i] * D
                        last = nc.gpsimd.tensor_tensor(
                            out_sb[own][:, a:a + w], t_sb[t_buf(t, h, n)][:, at:at + w],
                            x_sb[own][:, i + 1:F, :].rearrange("p f d -> p (f d)"), ALU.mult)
                        at += w
                    last.then_inc(gps_done, 1)

            over_stages(pool, stage)

        @block.scalar
        def _(act):
            act.dma_start(b_sb[:, :], b.rearrange("c e -> (c e)").rearrange("(r c) -> r c", r=BR)).then_inc(b_in, 16)

            def high_parts(t, h, n):
                item = list_of(t)[n]
                kind, m, off, _ = item
                src, high, _ = split_views(item, t, h)
                if kind == "W":
                    for c, (lo, _) in enumerate(W_LOADS):
                        if m == lo:
                            act.wait_ge(w_in[c], 16)
                    if m >= W_BUFS:
                        act.wait_ge(filled, upto(t, is_item, find(FIRST, "W", m - W_BUFS)))
                    nc.scalar.activation(high, src, ACT.Copy).then_inc(w_high_done, 1)
                    return
                if kind == "X":
                    if m == 0:
                        act.wait_ge(x_in[(h + off) % 2], 16)
                elif m == 0:
                    if same(t, 1):
                        act.wait_ge(next_in, 16)
                    else:
                        act.wait_ge(moved, t)
                earlier = [i for i in range(n) if is_x(list_of(t)[i]) and list_of(t)[i][1] == m]
                if earlier:
                    act.wait_ge(filled, upto(t, is_item, earlier[-1]))
                elif not same(t, 1) and m == 0:
                    act.wait_ge(filled, before(t, is_item))
                nc.scalar.activation(high, src, ACT.Copy).then_inc(high_done, 1)

            def stage(t, k, h):
                todo = list_of(t)
                copy_at = FIRST_COPY_AT if same(t, 1) else COPY_AT
                if same(t, 1):
                    for n in range(max(AHEAD, W_HIGH_AHEAD)):
                        if n < W_HIGH_AHEAD and is_w(todo[n]) or n < AHEAD and is_x(todo[n]):
                            high_parts(t, h, n)
                for n, item in enumerate(todo):
                    if n == copy_at and not same(t, TILES - 1):
                        if same(t, 1):
                            end = find(FIRST, "M", len(UNITS) - 1, -1)
                            act.wait_ge(vec_done, upto(t, by_vec, end))
                            act.wait_ge(gps_done, upto(t, by_gps, end))
                            act.wait_ge(low_done, sum(map(is_x, FIRST)))
                        else:
                            act.wait_ge(vec_done, before(t, by_vec))
                            act.wait_ge(gps_done, before(t, by_gps))
                        act.wait_ge(next_in, t * 16)
                        nc.scalar.activation(x_sb[1 - h][:, :, :], x_next[:, :, :], ACT.Copy).then_inc(moved, 1)
                        if not same(t, TILES - 2):
                            act.wait_ge(moved, t)
                            act.dma_start(x_next[:, :, :].rearrange("p f d -> p (f d)"),
                                          x_rows[t + 2, :, :]).then_inc(next_in, 16)
                    if n + W_HIGH_AHEAD < len(todo) and is_w(todo[n + W_HIGH_AHEAD]):
                        high_parts(t, h, n + W_HIGH_AHEAD)
                    if n + AHEAD < len(todo) and is_x(todo[n + AHEAD]):
                        high_parts(t, h, n + AHEAD)
                    if not by_act(item):
                        continue
                    s = n % SLOTS
                    act.wait_ge(filled, upto(t, is_item, n))
                    if item[0] != "M":
                        src, dst = empty_views(item, s, h)
                    else:
                        lo, hi, _ = UNITS[item[1]]
                        if not same(upto(t, by_gps, n), 1) and not same(upto(t, by_gps, n), 2):
                            act.wait_ge(gps_done, upto(t, by_gps, n) - 2)
                        w = pairs_of(lo, hi) * D
                        src, dst = slot[s][:, 0:w], t_sb[t_buf(t, h, n)][:, 0:w]
                    nc.scalar.activation(dst, src, ACT.Copy).then_inc(act_done, 1)

            over_stages(act, stage)

        @block.vector
        def _(dve):
            nc.vector.memset(out_sb[0][:, 0:BANK // 2], 0.0).then_inc(warm_set, 1)
            dve.wait_ge(ident_set, 2)
            nc.vector.tensor_copy(ident_r[:, :], ident[:, :]).then_inc(ident_set, 1)
            nc.vector.memset(bias_rows[:, 0:ZERO_AT].bitcast(fp32), 0.0).then_inc(bias_zero, 1)

            def split_bias():
                dve.wait_ge(b_in, 16)
                nc.vector.tensor_copy(b_parts[:, 0, :], b_sb[:, :]).then_inc(b_split, 1)
                dve.wait_ge(b_split, 1)
                nc.vector.tensor_tensor(b_rest[:, :], b_sb[:, :], b_parts[:, 0, :], ALU.subtract).then_inc(b_split, 1)
                dve.wait_ge(b_split, 2)
                nc.vector.tensor_copy(b_parts[:, 1, :], b_rest[:, :]).then_inc(b_split, 1)
                dve.wait_ge(b_split, 3)
                nc.vector.tensor_tensor(b_parts[:, 2, :], b_rest[:, :], b_parts[:, 1, :], ALU.subtract)\
                    .then_inc(b_split, 1)

            def low_parts(t, h, n):
                item = list_of(t)[n]
                if is_w(item):
                    dve.wait_ge(w_high_done, item[1] + 1)
                    done = w_low_vec
                else:
                    dve.wait_ge(high_done, upto(t, is_x, n))
                    done = low_done
                src, high, low = split_views(item, t, h)
                nc.vector.tensor_tensor(low, src, high.bitcast(fp32), ALU.subtract).then_inc(done, 1)

            def stage(t, k, h):
                todo = list_of(t)
                if same(t, 1):
                    for n in range(max(AHEAD - 1, W_LOW_AHEAD)):
                        if n < W_LOW_AHEAD and is_w(todo[n]) and low_by_vec(todo[n][1]) or n < AHEAD - 1 and is_x(todo[n]):
                            low_parts(t, h, n)
                else:
                    dve.wait_ge(moved, t - 1)
                freed, seen = set(), set()
                for n, item in enumerate(todo):
                    if n + W_LOW_AHEAD < len(todo) and is_w(todo[n + W_LOW_AHEAD]) and low_by_vec(todo[n + W_LOW_AHEAD][1]):
                        low_parts(t, h, n + W_LOW_AHEAD)
                    if n + AHEAD - 1 < len(todo) and is_x(todo[n + AHEAD - 1]):
                        low_parts(t, h, n + AHEAD - 1)
                    if not by_vec(item):
                        continue
                    s = n % SLOTS
                    dve.wait_ge(filled, upto(t, is_item, n))
                    if item[0] != "M":
                        src, dst = empty_views(item, s, h)
                        nc.vector.tensor_copy(dst, src).then_inc(vec_done, 1)
                        continue
                    if over_raw(item):
                        raw_read(dve)
                    lo, hi, _ = UNITS[item[1]]
                    own = (h + item[2]) % 2
                    if same(t, 1) and own not in seen:
                        seen.add(own)
                        dve.wait_ge(x_in[own], 16)
                    at = 0
                    for i in range(lo, hi):
                        if not same(k, 0) and chunk_of[i] not in freed:
                            freed.add(chunk_of[i])
                            dve.wait_ge(stored[h][chunk_of[i]], (k + extra[chunk_of[i]]) * 16)
                        w = pairs_of(i, i + 1) * D
                        a = first_pair[i] * D
                        last = nc.vector.tensor_tensor(
                            out_sb[own][:, a:a + w], slot[s][:, at:at + w],
                            x_sb[own][:, i + 1:F, :].rearrange("p f d -> p (f d)"), ALU.mult)
                        at += w
                    last.then_inc(vec_done, 1)

            split_bias()
            over_stages(dve, stage)

        @block.tensor
        def _(pe):
            pe.wait_ge(ones_set, 2)
            pe.wait_ge(warm_set, 1)
            for n in range(WARM_UP):
                nc.tensor.matmul(slot[0][:, 0:BANK], ones[:, :], out_sb[0][:, 0:BANK // 2].bitcast(bf16),
                                 start=True, stop=True)
            pe.wait_ge(ident_set, 3)

            def slot_free(t, n):
                v = n - SLOTS
                while v >= 0 and list_of(t)[v] is None:
                    v -= SLOTS
                if v < 0 and same(t, 1):
                    return
                prev = list_of(t)[v] if v >= 0 else REST[v]
                if by_vec(prev):
                    pe.wait_ge(vec_done, upto(t, by_vec, v))
                else:
                    pe.wait_ge(act_done, upto(t, by_act, v))

            def turn(item, s, h):
                kind, m, _, _ = item
                if kind == "W":
                    blocks = [W_parts[m % W_BUFS][0:w_rows(m), e, :, :] for e in range(EG)]
                else:
                    blocks = [x_parts[:, i, :, :] for i in range(*PIECES[m])]
                for n, parts in enumerate(blocks):
                    parts = parts.rearrange("p r d -> p (r d)")
                    last = nc.tensor.matmul(slot[s][:, n * P:(n + 1) * P], parts, ident_r[0:parts.shape[0], :],
                                            start=True, stop=True)
                last.then_inc(filled, 1)

            def products(item, s, h):
                lo, hi, _ = UNITS[item[1]]
                own = (h + item[2]) % 2
                a0, w = first_pair[lo] * D, pairs_of(lo, hi) * D
                for bank in range(0, w, BANK):
                    end = min(bank + BANK, w)
                    nc.tensor.matmul(slot[s][:, bank:end], ones[:, :], bias_rows[:, a0 + bank:a0 + end],
                                     start=True, stop=False)
                    for i in range(lo, hi):
                        a = max(first_pair[i] * D - a0, bank)
                        z = min(first_pair[i + 1] * D - a0, end)
                        if a < z:
                            last = nc.tensor.matmul(slot[s][:, a:z], x_stack[own][:, i * P:(i + 1) * P],
                                                    W_stack[:, a0 + a:a0 + z], start=False, stop=(z == end))
                last.then_inc(filled, 1)

            def stage(t, k, h):
                todo = list_of(t)
                turned = set()
                for n, item in enumerate(todo):
                    if item is None:
                        continue
                    slot_free(t, n)
                    if is_w(item):
                        m = item[1]
                        if low_by_vec(m):
                            pe.wait_ge(w_low_vec, sum(map(low_by_vec, range(m + 1))))
                        else:
                            pe.wait_ge(w_low_gps, m + 1 - sum(map(low_by_vec, range(m + 1))))
                        turn(item, n % SLOTS, h)
                        continue
                    if is_x(item):
                        pe.wait_ge(low_done, upto(t, is_x, n))
                        turn(item, n % SLOTS, h)
                        continue
                    lo, hi, _ = UNITS[item[1]]
                    for p, (a, z) in enumerate(PIECES):
                        if a < hi and lo < z and (p, item[2]) not in turned:
                            turned.add((p, item[2]))
                            if same(t, 1):
                                pe.wait_ge(act_done, upto(t, by_act, find(FIRST, "X", p, item[2])))
                            else:
                                pe.wait_ge(act_done, upto(t, by_act, find(REST, "T", p) - len(REST)))
                    if same(t, 1):
                        done = find(FIRST, "W", (first_pair[hi] - 1) // W_PAIRS)
                        if upto(t, by_vec, done):
                            pe.wait_ge(vec_done, upto(t, by_vec, done))
                        if upto(t, by_act, done):
                            pe.wait_ge(act_done, upto(t, by_act, done))
                        if item[:3] == ("M", 0, -1):
                            pe.wait_ge(bias_in, 3 * 16)
                    products(item, n % SLOTS, h)

            over_stages(pe, stage)


_INS = ['r_x', 'L0_rec_W', 'L0_rec_b']


def kernel(**inputs):
    import numpy as _np
    import concourse.bacc as _bacc
    from concourse import mybir as _mybir
    from concourse.bass_utils import run_bass_kernel_spmd as _run

    nc = _bacc.Bacc("TRN2", target_bir_lowering=False, num_devices=1)
    arrays, args = {}, []
    for name in _INS:
        a = _np.ascontiguousarray(inputs[name])
        arrays[f"in_{name}_dram"] = a
        args.append(nc.dram_tensor(f"in_{name}_dram", a.shape, _mybir.dt.from_np(a.dtype), kind="ExternalInput").ap())
    batch, _, dim = inputs['r_x'].shape
    shape = (batch, inputs['L0_rec_W'].shape[0], dim)
    out = nc.dram_tensor("out_0_dram", shape, _mybir.dt.float32, kind="ExternalOutput").ap()
    pairwise_bilinear_kernel(nc, *args, out)
    r = _run(nc, [arrays], core_ids=[0])
    return r.results[0]["out_0_dram"]
```
